# Optimizing a Trainium2 kernel written in Bass

```python
import numpy as np
import jax
import jax.numpy as jnp

def _softmax(x, axis=-1):
    return jax.nn.softmax(x, axis=axis)

def _gelu(x):
    return jax.nn.gelu(x, approximate=True)

def _silu(x):
    return jax.nn.silu(x)

def _sigmoid(x):
    return jax.nn.sigmoid(x)

def _layernorm(x, axis=-1, eps=1e-05):
    m = jnp.mean(x, axis=axis, keepdims=True)
    v = jnp.var(x, axis=axis, keepdims=True)
    return (x - m) / jnp.sqrt(v + eps)

def _scatter_add(tgt, idx, src, axis=0):
    return tgt.at[idx].add(src)

def _segment_sum(src, seg, n):
    return jax.ops.segment_sum(src, seg, n)
kernel_name = 'mk_gnn_resnorm_d2_gnn_r32_c6c952'

def setup_inputs(seed: int=0):
    np.random.seed(seed)
    _w = jnp.asarray

    def _rec_inputs():
        import jax
        import jax.numpy as jnp
        _gk = jax.random.key(seed)
        x = -0.0003713 + 1 * jax.random.normal(jax.random.fold_in(_gk, 1), (50000, 128), jnp.float32)
        src = jax.random.randint(jax.random.fold_in(_gk, 2), (50000,), 0, 50000, jnp.int32)
        dst = jnp.minimum((50000 * jax.random.uniform(jax.random.fold_in(_gk, 3), (50000,)) ** 2.0).astype(jnp.int32), 49999)
        _o = jnp.argsort(dst, stable=True)
        src = src[_o]
        dst = dst[_o]
        edge_attr_8 = jax.random.uniform(jax.random.fold_in(_gk, 12), (50000, 8), jnp.float32, 0.0, 1)
        edge_weight = jax.random.uniform(jax.random.fold_in(_gk, 14), (50000,), jnp.float32, 0.0, 0.999998)
        edge_weight_n2 = jax.random.uniform(jax.random.fold_in(_gk, 15), (50000,), jnp.float32, 0.0, 0.999998)
        edge_weight1 = 0.00121237 + 1.00026 * jax.random.normal(jax.random.fold_in(_gk, 16), (50000, 1), jnp.float32)
        return (x, src, dst, edge_attr_8, edge_weight, edge_weight_n2, edge_weight1)
    x, src, dst, edge_attr_8, edge_weight, edge_weight_n2, edge_weight1 = _rec_inputs()

    def _L0_gnn_setup():
        import jax, jax.numpy as jnp
        import numpy as np
        N, E = (3125, 50000)
        NODE_DIM, EDGE_DIM, NUM_BASIS, LMAX = (128, 128, 8, 0)
        NUM_SH = (LMAX + 1) ** 2
        key = jax.random.key(seed)
        ks = jax.random.split(key, 12)
        inp = {'node_feats': jax.random.normal(ks[0], (N, NODE_DIM), dtype=jnp.float32), 'edge_index': jax.random.randint(ks[1], (2, E), 0, N, dtype=jnp.int64), 'edge_rbf': jax.random.uniform(ks[2], (E, NUM_BASIS), dtype=jnp.float32), 'edge_sh': jax.random.normal(ks[3], (E, NUM_SH), dtype=jnp.float32), 'W1': jax.random.normal(ks[4], (NUM_BASIS, EDGE_DIM), dtype=jnp.float32) / np.sqrt(NUM_BASIS), 'b1': jnp.zeros((EDGE_DIM,), dtype=jnp.float32), 'W2': jax.random.normal(ks[5], (EDGE_DIM, NODE_DIM * (LMAX + 1)), dtype=jnp.float32) / np.sqrt(EDGE_DIM), 'b2': jnp.zeros((NODE_DIM * (LMAX + 1),), dtype=jnp.float32), 'Wself': jax.random.normal(ks[6], (NODE_DIM, NODE_DIM), dtype=jnp.float32) / np.sqrt(NODE_DIM), 'bself': jnp.zeros((NODE_DIM,), dtype=jnp.float32), 'Wcat': jax.random.normal(ks[7], (2 * NODE_DIM, NODE_DIM), dtype=jnp.float32) / np.sqrt(2 * NODE_DIM), 'bcat': jnp.zeros((NODE_DIM,), dtype=jnp.float32)}
        return inp
    _L0_gnn_all = _L0_gnn_setup()
    _L0_gnn_in = {k: v for k, v in _L0_gnn_all.items() if k in ('W1', 'b1', 'W2', 'b2', 'Wself', 'bself', 'Wcat', 'bcat')}
    del _L0_gnn_all

    def _L1_gnn_setup():
        import jax, jax.numpy as jnp
        import numpy as np
        N_NODES = 50000
        N_EDGES = 18750
        D_FEAT = 128
        key = jax.random.key(seed)
        k_h, k_src, k_dst, k_dt, k_norm = jax.random.split(key, 5)
        h = jax.random.normal(k_h, (N_NODES, D_FEAT), dtype=jnp.float32)
        src = jax.random.randint(k_src, (N_EDGES,), 0, N_NODES, dtype=jnp.int32)
        dst = jax.random.randint(k_dst, (N_EDGES,), 0, N_NODES, dtype=jnp.int32)
        dt = jax.random.uniform(k_dt, (N_EDGES,), dtype=jnp.float32) * 10.0
        norm = jax.random.uniform(k_norm, (N_EDGES,), dtype=jnp.float32)
        decay_lam = jnp.full((1,), 0.1, dtype=jnp.float32)
        return {'h': h, 'src': src, 'dst': dst, 'dt': dt, 'norm': norm, 'decay_lam': decay_lam}
    _L1_gnn_all = _L1_gnn_setup()
    _L1_gnn_in = {k: v for k, v in _L1_gnn_all.items() if k in ('decay_lam',)}
    del _L1_gnn_all
    return {'x': x, 'src': src, 'dst': dst, 'edge_attr_8': edge_attr_8, 'edge_weight': edge_weight, 'edge_weight_n2': edge_weight_n2, 'edge_weight1': edge_weight1, 'L0_gnn_W1': _L0_gnn_in['W1'], 'L0_gnn_b1': _L0_gnn_in['b1'], 'L0_gnn_W2': _L0_gnn_in['W2'], 'L0_gnn_b2': _L0_gnn_in['b2'], 'L0_gnn_Wself': _L0_gnn_in['Wself'], 'L0_gnn_bself': _L0_gnn_in['bself'], 'L0_gnn_Wcat': _L0_gnn_in['Wcat'], 'L0_gnn_bcat': _L0_gnn_in['bcat'], 'L1_gnn_decay_lam': _L1_gnn_in['decay_lam']}

def reference(x, src, dst, edge_attr_8, edge_weight, edge_weight_n2, edge_weight1, L0_gnn_W1, L0_gnn_b1, L0_gnn_W2, L0_gnn_b2, L0_gnn_Wself, L0_gnn_bself, L0_gnn_Wcat, L0_gnn_bcat, L1_gnn_decay_lam):
    import jax
    import jax.numpy as jnp

    def _L0_gnn_ref(node_feats, edge_index, edge_rbf, edge_sh, W1, b1, W2, b2, Wself, bself, Wcat, bcat):
        import jax, jax.numpy as jnp
        import numpy as np
        N, E = (3125, 50000)
        NODE_DIM, EDGE_DIM, NUM_BASIS, LMAX = (128, 128, 8, 0)
        NUM_SH = (LMAX + 1) ** 2
        row, col = (edge_index[0], edge_index[1])
        n_nodes = node_feats.shape[0]
        h = jax.nn.silu(edge_rbf @ W1 + b1)
        weights = (h @ W2 + b2).reshape(-1, NODE_DIM, LMAX + 1)
        node_j = node_feats[col]
        messages = (node_j[:, :, None] * weights).sum(axis=-1)
        aggregated = jax.ops.segment_sum(messages, row, num_segments=n_nodes)
        self_out = node_feats @ Wself + bself
        combined = jnp.concatenate([self_out, aggregated], axis=-1)
        return combined @ Wcat + bcat

    def _L1_gnn_ref(h, src, dst, dt, norm, decay_lam):
        import jax, jax.numpy as jnp
        import numpy as np
        N_NODES = 50000
        N_EDGES = 18750
        D_FEAT = 128
        lam = jax.nn.relu(decay_lam[0]) + 0.0001
        w = norm * jnp.exp(-lam * dt)
        m = h[src] * w[:, None]
        h_new = jax.ops.segment_sum(m, dst, num_segments=h.shape[0])
        return h_new
    edge_index = jnp.stack([src, dst])
    x = _layernorm(x + _L0_gnn_ref(x, edge_index, edge_attr_8, edge_weight1, L0_gnn_W1, L0_gnn_b1, L0_gnn_W2, L0_gnn_b2, L0_gnn_Wself, L0_gnn_bself, L0_gnn_Wcat, L0_gnn_bcat), axis=-1)
    x = _layernorm(x + _L1_gnn_ref(x, src, dst, edge_weight, edge_weight_n2, L1_gnn_decay_lam), axis=-1)
    return x

_drawn_inputs = setup_inputs


def setup_inputs(seed=0):
    import zlib

    import numpy as np

    out = dict(_drawn_inputs(seed))
    spreads = {'L0_gnn_b1': (0.0, 0.1),
     'L0_gnn_b2': (0.0, 0.1),
     'L0_gnn_bself': (0.0, 0.1),
     'L0_gnn_bcat': (0.0, 0.1)}
    factors = {'edge_weight': 5.93}
    for name, (base, spread) in spreads.items():
        noise = np.random.default_rng([zlib.crc32(name.encode()), seed]).standard_normal(out[name].shape)
        drawn = base * np.exp(spread * noise) if base else spread * noise
        out[name] = jnp.asarray(drawn.astype(out[name].dtype))
    for name, factor in factors.items():
        out[name] = (out[name] * factor).astype(out[name].dtype)
    return out
```

```python
from contextlib import ExitStack

import concourse.bass as bass
from concourse import mybir

N = 50000
E = 50000
D = 128
R = 8
P = 128
Q = 4
W = Q * P
NQ = -(-N // (2 * W)) * 2
NT = NQ * Q
NPAD = NQ * W
LASTP = (N - (NQ - 1) * W) // Q
ZCH = NPAD * D // (P * 1024)
EPS = 1e-5
LAM0 = 1e-4


class EdgeSems:

    def __init__(self, sem, tag):
        self.hid_ps = sem(f"{tag}_hid_ps")
        self.hid_ready = sem(f"{tag}_hid_ready")
        self.w_ready = sem(f"{tag}_w_ready")
        self.msg_ready = sem(f"{tag}_msg_ready")
        self.eq_ready = sem(f"{tag}_eq_ready")
        self.sum_ready = sem(f"{tag}_sum_ready")
        self.sum_copied = sem(f"{tag}_sum_copied")
        self.idx_ready = sem(f"{tag}_idx_ready")
        self.gidx_ready = sem(f"{tag}_gidx_ready")
        self.key_in = [sem(f"{tag}_key_in{h}") for h in range(2)]
        self.ea_in = [sem(f"{tag}_ea_in{h}") for h in range(2)]
        self.gathered = [sem(f"{tag}_gathered{h}") for h in range(2)]
        self.added = [sem(f"{tag}_added{j}") for j in range(Q)]


class NodeSems:

    def __init__(self, sem, tag):
        self.var_ready = sem(f"{tag}_var_ready")
        self.std_ready = sem(f"{tag}_std_ready")
        self.t_ready = sem(f"{tag}_t_ready")
        self.t_copied = sem(f"{tag}_t_copied")
        self.a_copied = sem(f"{tag}_a_copied")
        self.u_ready = sem(f"{tag}_u_ready")
        self.y_ready = sem(f"{tag}_y_ready")
        self.done = sem(f"{tag}_done")
        self.x_in = [sem(f"{tag}_x_in{h}") for h in range(2)]
        self.stored = [sem(f"{tag}_stored{h}") for h in range(2)]


def build(nc, x, src, dst, ea, ew, ewn, w1, b1, w2, b2, wself_t, bself, wcat, bcat, lam,
          srcr, dstr, ident_in, tri_in, trash_in, out):
    f32, i32 = mybir.dt.float32, mybir.dt.int32
    ALU, ACT, AX = mybir.AluOpType, mybir.ActivationFunctionType, mybir.AxisListType
    acc = [[nc.dram_tensor(f"acc{l}_{j}", [NPAD, D], f32, kind="Internal").ap() for j in range(Q)] for l in range(2)]
    x1 = nc.dram_tensor("x1", [NPAD, D], f32, kind="Internal").ap()

    with ExitStack() as ctx:
        def sb(name, shape, dt=f32):
            return ctx.enter_context(nc.sbuf_tensor(name, shape, dt))

        def pb(name, shape):
            return ctx.enter_context(nc.psum_tensor(name, shape, f32))

        def sem(name):
            return ctx.enter_context(nc.semaphore(name))

        ident, tri = sb("ident", [P, P]), sb("tri", [P, P])
        w1_sb, w2_sb = sb("w1_sb", [R, P]), sb("w2_sb", [P, D])
        b1_sb, b2_sb = sb("b1_sb", [P, 1]), sb("b2_sb", [1, D])
        wself_sb = sb("wself_sb", [P, D])
        wtop, wbot = sb("wtop", [P, D]), sb("wbot", [P, D])
        bself_sb, bcat_sb = sb("bself_sb", [P, 1]), sb("bcat_sb", [1, D])
        comb, cbias = sb("comb", [P, D]), sb("cbias", [1, D])
        ones = sb("ones", [1, P])
        zero = sb("zero", [P, 1024])
        lam_sb = sb("lam_sb", [P, 1])
        srcc, dstc = sb("srcc", [P, NT], i32), sb("dstc", [P, NT], i32)
        ewc, ewnc, wl1 = sb("ewc", [P, NT]), sb("ewnc", [P, NT]), sb("wl1", [P, NT])
        trash = sb("trash", [P, 1])
        H = range(2)
        keyrow = [sb(f"keyrow{h}", [P, W], i32) for h in H]
        ea_sb = [sb(f"ea_sb{h}", [R, W]) for h in H]
        hid = [sb(f"hid{h}", [P, W]) for h in H]
        gath = [sb(f"gath{h}", [P, W]) for h in H]
        gidx = [sb(f"gidx{h}", [P, Q], i32) for h in H]
        sidx = [sb(f"sidx{h}", [P, Q], i32) for h in H]
        eq = [sb(f"eq{h}", [P, W]) for h in H]
        eqt = sb("eqt", [P, W])
        cnt, dup, key4, trm = (sb(n, [P, Q]) for n in ("cnt", "dup", "key4", "trm"))
        msg = [sb(f"msg{h}", [P, W]) for h in H]
        summed = [sb(f"summed{h}", [P, W]) for h in H]
        xq = [sb(f"xq{h}", [P, W]) for h in H]
        aq = [sb(f"aq{h}", [P, Q, W]) for h in H]
        xt = [sb(f"xt{h}", [P, W]) for h in H]
        at = [sb(f"at{h}", [P, W]) for h in H]
        yq = [sb(f"yq{h}", [P, W]) for h in H]
        oq = [sb(f"oq{h}", [P, W]) for h in H]
        stats, mv, rstd = sb("stats", [P, Q, 6]), sb("mv", [P, Q, 2]), sb("rstd", [P, Q])

        std, eps = sb("std", [P, Q]), sb("eps", [P, 1])
        ps_h = [pb(f"ps_h{h}", [P, W]) for h in H]
        ps_w = [pb(f"ps_w{h}", [P, W]) for h in H]
        ps_s = [pb(f"ps_s{h}", [P, W]) for h in H]
        ps_c = pb("ps_c", [P, W])

        s_load, s_zero, s_const, s_wl1 = sem("s_load"), sem("s_zero"), sem("s_const"), sem("s_wl1")
        s_seen = sem("s_seen")
        s_dveseen = sem("s_dveseen")
        s_comb, s_combs, s_exp = sem("s_comb"), sem("s_combs"), sem("s_exp")
        dve_order = sem("dve_order")

        edge = [EdgeSems(sem, f"e{l}") for l in range(2)]
        node = [NodeSems(sem, f"n{l}") for l in range(2)]

        NLOAD = 17
        block = ctx.enter_context(nc.Block())

        def rows(ap, q):
            return ap[bass.ds(q * W, W), :].rearrange("(p j) d -> p (j d)", j=Q)

        @block.sync
        def _(sp):
            for a, b in ((ident, ident_in), (tri, tri_in), (w1_sb, w1), (w2_sb, w2),
                         (b1_sb, b1.rearrange("(p o) -> p o", o=1)), (b2_sb, b2.rearrange("(o d) -> o d", o=1)),
                         (wself_sb, wself_t), (wtop, wcat[0:D, :]), (wbot, wcat[D:2 * D, :]),
                         (bself_sb, bself.rearrange("(p o) -> p o", o=1)),
                         (bcat_sb, bcat.rearrange("(o d) -> o d", o=1)),
                         (lam_sb, lam.rearrange("(o d) -> o d", o=1).to_broadcast([P, 1])),
                         (srcc, src), (dstc, dst), (ewc, ew), (ewnc, ewn), (trash, trash_in)):
                sp.dma_start(a[:, :], b).then_inc(s_load, 16)
            sp.wait_ge(s_const, 1)
            for a in acc[0] + acc[1]:
                flat = a.rearrange("n d -> (n d)").rearrange("(c p m) -> c p m", p=P, m=1024)
                with sp.Fori(0, flat.shape[0]) as c:
                    sp.dma_start(flat[bass.ds(c, 1), :, :].rearrange("c p m -> p (c m)"), zero[:, :]).then_inc(s_zero, 16)

            def edge_loads(l, keys):
                e = edge[l]
                keyv = keys.rearrange("p t -> (p t)")
                with sp.Fori(0, NQ // 2) as i:
                    for h in H:
                        q = i * 2 + h
                        sp.wait_ge(e.eq_ready, q + 1)
                        sp.dma_start(keyrow[h][:, :], keys[bass.ds(q, 1), :].to_broadcast([P, W])).then_inc(e.key_in[h], 16)
                        if l == 0:
                            sp.wait_ge(e.hid_ps, q + 1)
                            sp.dma_start(ea_sb[h][:, :], ea[:, bass.ds(q * W, W)]).then_inc(e.ea_in[h], 16)

            def node_loads(l, xin):
                n = node[l]
                with sp.Fori(0, NQ // 2 - 1) as i:
                    for h in H:
                        q = i * 2 + h
                        sp.wait_ge(n.done, q + 1)
                        sp.dma_start(xq[h][:, :], rows(xin, q)).then_inc(n.x_in[h], 16)
                        for k in range(Q):
                            sp.dma_start(aq[h][:, k, :], rows(acc[l][k], q)).then_inc(n.x_in[h], 16)
                for h in H:
                    q = NQ - 2 + h
                    sp.wait_ge(n.done, q + 1)
                    m = LASTP if h else P
                    sp.dma_start(xq[h][0:m, :], xin[q * W:q * W + m * Q, :].rearrange("(p j) d -> p (j d)", j=Q)).then_inc(n.x_in[h], 16)
                    for k in range(Q):
                        sp.dma_start(aq[h][:, k, :], rows(acc[l][k], q)).then_inc(n.x_in[h], 16)

            edge_loads(0, srcr)
            for j in range(Q):
                sp.wait_ge(edge[0].added[j], 16 * NQ)
            node_loads(0, x)
            edge_loads(1, dstr)
            for j in range(Q):
                sp.wait_ge(edge[1].added[j], 16 * NQ)
            node_loads(1, x1)

        @block.gpsimd
        def _(pool):
            def dma_after_waits():
                pool.sem_inc(s_seen, 1)

            def gather(l, q, h, table):
                e = edge[l]
                pool.wait_ge(e.gidx_ready, q + 1)
                pool.wait_ge(e.msg_ready, q + 1)
                dma_after_waits()
                for j in range(Q):
                    pool.indirect_dma_start(out=gath[h][:, j * P:(j + 1) * P], out_offset=None, in_=table,
                                            in_offset=bass.IndirectOffsetOnAxis(ap=gidx[h][:, j:j + 1], axis=0)
                                            ).then_inc(e.gathered[h], 16)

            def scatter(l, q, h, first=False):
                e = edge[l]
                pool.wait_ge(e.sum_copied, q + 3)
                pool.wait_ge(e.idx_ready, q + 1)
                for j in range(Q):
                    if not first:
                        pool.wait_ge(e.added[j], q * 16)
                    dma_after_waits()
                    pool.indirect_dma_start(out=acc[l][j], out_offset=bass.IndirectOffsetOnAxis(ap=sidx[h][:, j:j + 1], axis=0),
                                            in_=summed[h][:, j * P:(j + 1) * P], in_offset=None,
                                            compute_op=ALU.add).then_inc(e.added[j], 16)

            for l, table in ((0, x), (1, x1)):
                if l == 0:
                    pool.wait_ge(s_zero, 2 * Q * ZCH * 16)
                else:
                    for h in H:
                        pool.wait_ge(node[0].stored[h], 16 * (NQ // 2 + 1))
                gather(l, 0, 0, table)
                gather(l, 1, 1, table)
                scatter(l, 0, 0, first=True)
                with pool.Fori(1, NQ // 2) as i:
                    gather(l, i * 2, 0, table)
                    scatter(l, i * 2 - 1, 1)
                    gather(l, i * 2 + 1, 1, table)
                    scatter(l, i * 2, 0)
                scatter(l, NQ - 1, 1)

        @block.tensor
        def _(pe):
            mm = nc.tensor.matmul
            pe.sem_inc(edge[0].hid_ps, 2)
            pe.wait_ge(s_load, 16 * NLOAD)
            pe.wait_ge(s_const, 2)
            mm(ps_c[:, 0:D], wself_sb[:, :], wtop[:, :], start=True, stop=True)
            mm(ps_c[0:1, D:2 * D], bself_sb[:, :], wtop[:, :], start=True, stop=True).then_inc(s_comb, 1)

            def edges(l, q, h):
                e = edge[l]
                if l == 0:
                    pe.wait_ge(e.ea_in[h], q * 8 + 16 - 8 * h)
                    pe.wait_ge(e.hid_ready, q + 1)
                    mm(ps_h[h][:, :], w1_sb[:, :], ea_sb[h][:, :], start=True, stop=True).then_inc(e.hid_ps, 1)
                    pe.wait_ge(e.hid_ready, q + 3)
                    pe.wait_ge(e.msg_ready, q + 1)
                    for j in range(Q):
                        c = slice(j * P, (j + 1) * P)
                        mm(ps_w[h][:, c], hid[h][:, c], w2_sb[:, :], start=True, stop=False)
                        last = mm(ps_w[h][:, c], ones[:, :], b2_sb[:, :], start=False, stop=True)
                    last.then_inc(e.w_ready, 1)
                pe.wait_ge(e.msg_ready, q + 3)
                pe.wait_ge(e.eq_ready, q + 3)
                pe.wait_ge(e.sum_copied, q + 1)
                for j in range(Q):
                    c = slice(j * P, (j + 1) * P)
                    last = mm(ps_s[h][:, c], eq[h][:, c], msg[h][:, c], start=True, stop=True)
                last.then_inc(e.sum_ready, 1)

            def nodes(l, q, h):
                n = node[l]
                pe.wait_ge(n.x_in[h], (q - h) * 8 * (Q + 1) + 16 * (Q + 1))
                pe.wait_ge(n.y_ready, q + 1)
                if l == 0:
                    pe.wait_ge(n.t_copied, q + 1)
                    pe.wait_ge(n.a_copied, q + 1)
                    for j in range(Q):
                        c = slice(j * P, (j + 1) * P)
                        mm(ps_h[h][:, c], xq[h][:, c], ident[:, :], start=True, stop=True)
                        for k in range(Q):
                            last = mm(ps_w[h][:, c], aq[h][:, k, c], ident[:, :], start=(k == 0), stop=(k == Q - 1))
                    last.then_inc(n.t_ready, 1)
                    pe.wait_ge(n.t_copied, q + 3)
                    pe.wait_ge(n.a_copied, q + 3)
                    for j in range(Q):
                        c = slice(j * P, (j + 1) * P)
                        mm(ps_s[h][:, c], xt[h][:, c], comb[:, :], start=True, stop=False)
                        mm(ps_s[h][:, c], at[h][:, c], wbot[:, :], start=False, stop=False)
                        last = mm(ps_s[h][:, c], ones[:, :], cbias[:, :], start=False, stop=True)
                else:
                    for k in range(Q):
                        last = mm(ps_s[h][:, :], ident[:, :], aq[h][:, k, :], start=(k == 0), stop=(k == Q - 1))
                last.then_inc(n.u_ready, 1)

            for l in range(2):
                with pe.Fori(0, NQ // 2) as i:
                    for h in H:
                        edges(l, i * 2 + h, h)
                if l == 0:
                    pe.wait_ge(s_combs, 1)
                with pe.Fori(0, NQ // 2) as i:
                    for h in H:
                        nodes(l, i * 2 + h, h)

        @block.scalar
        def _(act):
            act.wait_ge(s_load, 16 * NLOAD)
            act.wait_ge(s_wl1, 1)
            nc.scalar.activation(wl1[:, :], ewc[:, :], ACT.Exp, scale=lam_sb[:, 0:1]).then_inc(s_exp, 1)
            for l in range(2):
                e, n = edge[l], node[l]
                act.sem_inc(e.hid_ready, 2)
                act.sem_inc(e.sum_copied, 2)
                act.sem_inc(n.t_copied, 2)
                for h in H:
                    act.sem_inc(n.stored[h], 16)
            for l in range(2):
                e, n = edge[l], node[l]

                def edge_quad(q, h, first=False):
                    if l == 0:
                        act.wait_ge(e.hid_ps, q + 3)
                        nc.scalar.activation(hid[h][:, :], ps_h[h][:, :], ACT.Silu, bias=b1_sb[:, 0:1]).then_inc(e.hid_ready, 1)
                    act.wait_ge(e.sum_ready, q + 1)
                    if not first:
                        for j in range(Q):
                            act.wait_ge(e.added[j], q * 16 - 16)
                    nc.scalar.copy(summed[h][:, :], ps_s[h][:, :]).then_inc(e.sum_copied, 1)

                for h in H:
                    edge_quad(h, h, first=True)
                with act.Fori(1, NQ // 2) as i:
                    for h in H:
                        edge_quad(i * 2 + h, h)

                def node_quad(q, h, rows_out):
                    if l == 0:
                        act.wait_ge(n.t_ready, q + 1)
                        nc.scalar.copy(xt[h][:, :], ps_h[h][:, :]).then_inc(n.t_copied, 1)
                    act.wait_ge(n.var_ready, q + 1)
                    nc.scalar.activation(std[:, :], mv[:, :, 1], ACT.Sqrt, bias=eps[:, 0:1]).then_inc(n.std_ready, 1)
                    act.wait_ge(n.done, q + 3)
                    m = P if rows_out is None else LASTP
                    to = x1 if l == 0 else out
                    if rows_out is None:
                        act.dma_start(rows(to, q), oq[h][:, :]).then_inc(n.stored[h], 16)
                    else:
                        act.dma_start(to[q * W:q * W + rows_out * Q, :].rearrange("(p j) d -> p (j d)", j=Q),
                                      oq[h][0:rows_out, :]).then_inc(n.stored[h], 16)

                with act.Fori(0, NQ // 2 - 1) as i:
                    for h in H:
                        node_quad(i * 2 + h, h, None)
                node_quad(NQ - 2, 0, P)
                node_quad(NQ - 1, 1, P if l == 0 else LASTP)
            for h in H:
                act.wait_ge(node[1].stored[h], 16 * (NQ // 2 + 1))

        @block.vector
        def _(dve):
            v = nc.vector
            done = [0]

            def link(ins, base=0):
                ins.then_inc(dve_order, 1)
                done[0] += 1
                dve.wait_ge(dve_order, base + done[0])

            link(v.memset(zero[:, :], 0.0))
            v.memset(zero[:, 0:1], 0.0).then_inc(s_const, 1)
            v.memset(eps[:, :], EPS)
            v.memset(ones[:, :], 1.0).then_inc(s_const, 1)
            for l in range(2):
                dve.sem_inc(edge[l].msg_ready, 2)
                dve.sem_inc(edge[l].eq_ready, 2)
                dve.sem_inc(node[l].a_copied, 2)
                dve.sem_inc(node[l].y_ready, 2)
                dve.sem_inc(node[l].done, 2)
            dve.wait_ge(s_load, 16 * NLOAD)
            link(v.tensor_scalar(lam_sb[:, :], lam_sb[:, :], 0.0, LAM0, ALU.max, ALU.add))
            v.tensor_scalar(lam_sb[:, :], lam_sb[:, :], -1.0, None, ALU.mult).then_inc(s_wl1, 1)
            dve.wait_ge(s_exp, 1)
            link(v.tensor_tensor(wl1[:, :], wl1[:, :], ewnc[:, :], ALU.mult))
            dve.wait_ge(s_comb, 1)
            v.tensor_copy(comb[:, :], ps_c[:, 0:D])
            v.tensor_tensor(cbias[:, :], ps_c[0:1, D:2 * D], bcat_sb[:, :], ALU.add).then_inc(s_combs, 1)

            def q3(ap):
                return ap.rearrange("p (j n) -> p j n", j=Q)

            for l in range(2):
                e, n = edge[l], node[l]
                gcol, scol = ((dstc, srcc), (srcc, dstc))[l]

                def next_gidx(q, h):
                    v.tensor_scalar(gidx[h][:, :], gcol[:, bass.ds(q * Q, Q)], N - 1, None, ALU.min).then_inc(e.gidx_ready, 1)

                LINKS = 6

                def edge_quad(q, h, base, first=False, last=False):
                    col = scol[:, bass.ds(q * Q, Q)]
                    if not last:
                        next_gidx(q + 1, 1 - h)
                    dve.wait_ge(e.key_in[h], q * 8 + 16 - 8 * h)
                    if not first:
                        dve.wait_ge(e.sum_ready, q - 1)
                    ins = v.tensor_tensor(q3(eq[h][:, :]), q3(keyrow[h][:, :]), col.unsqueeze(2).to_broadcast([P, Q, P]), ALU.is_equal)
                    link(ins, base)
                    dve.sem_inc(e.eq_ready, 1)
                    link(v.tensor_tensor(q3(eqt[:, :]), q3(eq[h][:, :]), tri[:, :].unsqueeze(1).to_broadcast([P, Q, P]), ALU.mult), base)
                    v.tensor_scalar(key4[:, :], col, 1.0, None, ALU.mult)
                    link(v.tensor_reduce(cnt[:, :], q3(eqt[:, :]), AX.X, ALU.add), base)
                    v.tensor_scalar(dup[:, :], cnt[:, :], 1.0, None, ALU.min)
                    link(v.tensor_scalar(trm[:, :], key4[:, :], -1.0, trash[:, 0:1], ALU.mult, ALU.add), base)
                    link(v.tensor_tensor(trm[:, :], trm[:, :], dup[:, :], ALU.mult), base)
                    if not first:
                        for j in range(Q):
                            dve.wait_ge(e.added[j], q * 16 - 16)
                    v.tensor_tensor(sidx[h][:, :], trm[:, :], key4[:, :], ALU.add).then_inc(e.idx_ready, 1)
                    dve.wait_ge(e.gathered[h], q * 32 + 64 - 32 * h)
                    if l == 0:
                        dve.wait_ge(e.w_ready, q + 1)
                        ins = v.tensor_tensor(msg[h][:, :], gath[h][:, :], ps_w[h][:, :], ALU.mult)
                    else:
                        ins = v.tensor_tensor(q3(msg[h][:, :]), q3(gath[h][:, :]),
                                              wl1[:, bass.ds(q * Q, Q)].unsqueeze(2).to_broadcast([P, Q, P]), ALU.mult)
                    ins.then_inc(e.msg_ready, 1)
                    link(v.tensor_copy(dup[0:1, 0:1], dup[0:1, 0:1]), base)

                def run(quad, lo, links):
                    start = done[0]
                    with dve.Fori(lo, NQ // 2 - 1) as i:
                        for h in H:
                            quad(i * 2 + h, h, (i - lo) * (2 * links))
                    assert done[0] - start == 2 * links, done[0] - start
                    done[0] = start + 2 * links * (NQ // 2 - 1 - lo)

                next_gidx(0, 0)
                for h in H:
                    edge_quad(h, h, 0, first=True)
                run(edge_quad, 1, LINKS)
                edge_quad(NQ - 2, 0, 0)
                edge_quad(NQ - 1, 1, 0, last=True)

                def node_quad(q, h, base):
                    if l == 0:
                        dve.wait_ge(n.t_ready, q + 1)
                        v.tensor_copy(at[h][:, :], ps_w[h][:, :]).then_inc(n.a_copied, 1)
                    dve.wait_ge(n.u_ready, q + 1)
                    ins = v.tensor_tensor(yq[h][:, :], xq[h][:, :], ps_s[h][:, :], ALU.add)
                    link(ins, base)
                    dve.sem_inc(n.y_ready, 1)
                    for j in range(Q):
                        ins = v.bn_stats(stats[:, j, :], yq[h][:, j * P:(j + 1) * P])
                    link(ins, base)
                    dve.sem_inc(s_dveseen, 1)
                    for j in range(Q):
                        ins = v.bn_aggr(mv[:, j, :], stats[:, j, :])
                    link(ins, base)
                    dve.sem_inc(n.var_ready, 1)
                    dve.wait_ge(n.std_ready, q + 1)
                    link(v.reciprocal(rstd[:, :], std[:, :]), base)
                    dve.wait_ge(n.stored[h], q * 8 + 16 - 8 * h)
                    for j in range(Q):
                        c = slice(j * P, (j + 1) * P)
                        ins = v.tensor_scalar(oq[h][:, c], yq[h][:, c], mv[:, j, 0:1], rstd[:, j:j + 1], ALU.subtract, ALU.mult)
                    link(ins, base)
                    dve.sem_inc(n.done, 1)

                run(node_quad, 0, 5)
                node_quad(NQ - 2, 0, 0)
                node_quad(NQ - 1, 1, 0)


_OUTS = [((N, D), "float32")]


def kernel(x, src, dst, edge_attr_8, edge_weight, edge_weight_n2, edge_weight1, L0_gnn_W1, L0_gnn_b1, L0_gnn_W2,
           L0_gnn_b2, L0_gnn_Wself, L0_gnn_bself, L0_gnn_Wcat, L0_gnn_bcat, L1_gnn_decay_lam):
    import numpy as np
    import concourse.bacc as bacc
    from concourse.bass_utils import run_bass_kernel_spmd

    def lay(a, fill):
        a = np.asarray(a)
        rows = np.full((NPAD,) + a.shape[1:], fill, a.dtype)
        rows[:E] = a
        return rows

    def columns(a):
        return np.ascontiguousarray(a.reshape(NT, P).T)

    s, d = lay(src, N), lay(dst, N)
    ins = {
        "x": np.asarray(x), "src": columns(s), "dst": columns(d),
        "ea": np.ascontiguousarray(lay(edge_attr_8, 0).T),
        "ew": columns(lay(edge_weight, 0)), "ewn": columns(lay(edge_weight_n2, 0)),
        "w1": np.asarray(L0_gnn_W1), "b1": np.asarray(L0_gnn_b1), "w2": np.asarray(L0_gnn_W2), "b2": np.asarray(L0_gnn_b2),
        "wself_t": np.ascontiguousarray(np.asarray(L0_gnn_Wself).T), "bself": np.asarray(L0_gnn_bself),
        "wcat": np.asarray(L0_gnn_Wcat), "bcat": np.asarray(L0_gnn_bcat), "lam": np.asarray(L1_gnn_decay_lam),
        "srcr": s.reshape(NQ, W), "dstr": d.reshape(NQ, W),
        "ident": np.eye(P, dtype=np.float32), "tri": np.tril(np.ones((P, P), np.float32), -1),
        "trash": (N + np.arange(P, dtype=np.float32)).reshape(P, 1),
    }
    nc = bacc.Bacc("TRN2", target_bir_lowering=False, num_devices=1)
    args = [nc.dram_tensor(f"in_{k}", a.shape, mybir.dt.from_np(a.dtype), kind="ExternalInput").ap() for k, a in ins.items()]
    out = nc.dram_tensor("out", (N, D), mybir.dt.float32, kind="ExternalOutput").ap()
    build(nc, *args, out)
    r = run_bass_kernel_spmd(nc, [{f"in_{k}": a for k, a in ins.items()}], core_ids=[0])
    return r.results[0]["out"]
```
